# Optimizing a Trainium2 kernel written in Bass

```python
import numpy as np
import jax
import jax.numpy as jnp

def _softmax(x, axis=-1):
    return jax.nn.softmax(x, axis=axis)

def _gelu(x):
    return jax.nn.gelu(x, approximate=True)

def _silu(x):
    return jax.nn.silu(x)

def _sigmoid(x):
    return jax.nn.sigmoid(x)

def _layernorm(x, axis=-1, eps=1e-05):
    m = jnp.mean(x, axis=axis, keepdims=True)
    v = jnp.var(x, axis=axis, keepdims=True)
    return (x - m) / jnp.sqrt(v + eps)

def _scatter_add(tgt, idx, src, axis=0):
    return tgt.at[idx].add(src)

def _segment_sum(src, seg, n):
    return jax.ops.segment_sum(src, seg, n)
kernel_name = 'mk_seq_preln_d2_jaxref_r8_f82ad9'

def setup_inputs(seed: int=0):
    np.random.seed(seed)
    _w = jnp.asarray

    def _L0_attn_setup():
        import jax, jax.numpy as jnp
        import numpy as np
        import math
        D_MODEL = 128
        N_HEADS = 16
        HEAD_DIM = D_MODEL // N_HEADS
        ROT_DIM = min(32, D_MODEL // 4)

        def _xavier(key, fan_in, fan_out):
            lim = math.sqrt(6.0 / (fan_in + fan_out))
            return jax.random.uniform(key, (fan_in, fan_out), jnp.float32, -lim, lim)
        key = jax.random.key(seed)
        ks = jax.random.split(key, 6)
        x = jax.random.normal(ks[0], (2, 256, D_MODEL), jnp.float32)
        Wq = _xavier(ks[1], D_MODEL, D_MODEL)
        Wk = _xavier(ks[2], D_MODEL, D_MODEL)
        Wv = _xavier(ks[3], D_MODEL, D_MODEL)
        Wr = _xavier(ks[4], D_MODEL, N_HEADS * ROT_DIM)
        Wo = _xavier(ks[5], D_MODEL, D_MODEL)
        z = jnp.zeros((D_MODEL,), jnp.float32)
        zr = jnp.zeros((N_HEADS * ROT_DIM,), jnp.float32)
        return {'x': x, 'Wq': Wq, 'bq': z, 'Wk': Wk, 'bk': z, 'Wv': Wv, 'bv': z, 'Wr': Wr, 'br': zr, 'Wo': Wo, 'bo': z}
    _L0_attn_in = _L0_attn_setup()

    def _L0_ffn_setup():
        import jax, jax.numpy as jnp
        import numpy as np
        B, L, H = (8, 256, 128)
        E, K, R = (8, 2, 64)

        def _gates(cls_tok, Wr):
            logits = cls_tok @ Wr.T
            top_vals, top_idx = jax.lax.top_k(logits, K)
            neg_inf = jnp.full_like(logits, -jnp.inf)
            rows = jnp.arange(logits.shape[0])[:, None]
            masked = neg_inf.at[rows, top_idx].set(top_vals)
            return jax.nn.softmax(masked, axis=-1)
        key = jax.random.key(seed)
        k1, k2, k3, k4 = jax.random.split(key, 4)
        x = jax.random.normal(k1, (B, L, H), dtype=jnp.float32)
        Wr = jax.random.normal(k2, (E, H), dtype=jnp.float32) * (1.0 / np.sqrt(H))
        A = jax.random.normal(k3, (E, R, H), dtype=jnp.float32) * (1.0 / np.sqrt(H))
        Bw = jax.random.normal(k4, (E, H, R), dtype=jnp.float32) * (1.0 / np.sqrt(R))
        return {'x': x, 'Wr': Wr, 'A': A, 'Bw': Bw}
    _L0_ffn_in = _L0_ffn_setup()

    def _L1_attn_setup():
        import jax, jax.numpy as jnp
        import numpy as np
        H = 8
        SPARSITY = 0.1
        key = jax.random.key(seed)
        ks = jax.random.split(key, 16)
        B, S, D = (2, 256, 128)
        g2 = H * H
        std = 0.02
        inp = {'x': jax.random.normal(ks[0], (B, S, D), dtype=jnp.float32), 'Wq': jax.random.normal(ks[1], (D, D)) * std, 'bq': jnp.zeros((D,)), 'Wk': jax.random.normal(ks[2], (D, D)) * std, 'bk': jnp.zeros((D,)), 'Wv': jax.random.normal(ks[3], (D, D)) * std, 'bv': jnp.zeros((D,)), 'Wo': jax.random.normal(ks[4], (D, D)) * std, 'bo': jnp.zeros((D,)), 'Wd': jax.random.normal(ks[5], (g2, g2)) * std, 'bd': jnp.zeros((g2,)), 'Wg': jax.random.normal(ks[6], (g2, D)) * std, 'bg': jnp.zeros((g2,)), 'Wgp': jax.random.normal(ks[7], (D, g2)) * std, 'bgp': jnp.zeros((D,))}
        return inp
    _L1_attn_in = _L1_attn_setup()

    def _L1_ffn_setup():
        import jax, jax.numpy as jnp
        import numpy as np
        B, L, M = (4, 256, 128)
        G, E = (8, 8)
        CAP_FACTOR = 2.0

        def _ffn_size(m, widening=8.0):
            f = int(widening * m) * 2 // 3
            return f + (8 - f) % 8
        H = _ffn_size(M)

        def _gating_top2(logits, C):
            Gd, Sd, Ed = logits.shape
            raw = jax.nn.softmax(logits, axis=-1)
            idx1 = jnp.argmax(raw, axis=-1)
            m1 = jax.nn.one_hot(idx1, Ed, dtype=logits.dtype)
            gate1 = jnp.sum(raw * m1, axis=-1)
            rest = raw * (1.0 - m1)
            idx2 = jnp.argmax(rest, axis=-1)
            m2 = jax.nn.one_hot(idx2, Ed, dtype=logits.dtype)
            gate2 = jnp.sum(rest * m2, axis=-1)
            p1 = jnp.cumsum(m1, axis=-2) - m1
            m1 = m1 * (p1 < C).astype(m1.dtype)
            p1 = jnp.sum(p1 * m1, axis=-1)
            m1_flat = jnp.sum(m1, axis=-1)
            m1_count = jnp.sum(m1, axis=-2)
            p2 = jnp.cumsum(m2, axis=-2) - m2 + m1_count[:, None, :]
            m2 = m2 * (p2 < C).astype(m2.dtype)
            p2 = jnp.sum(p2 * m2, axis=-1)
            m2_flat = jnp.sum(m2, axis=-1)
            gate1 = gate1 * m1_flat
            gate2 = gate2 * m2_flat
            c1 = (gate1[..., None] * jax.nn.one_hot(idx1, Ed, dtype=jnp.float32))[..., None] * jax.nn.one_hot(p1.astype(jnp.int32), C, dtype=jnp.float32)[:, :, None, :]
            c2 = (gate2[..., None] * jax.nn.one_hot(idx2, Ed, dtype=jnp.float32))[..., None] * jax.nn.one_hot(p2.astype(jnp.int32), C, dtype=jnp.float32)[:, :, None, :]
            combine = (c1 + c2).astype(logits.dtype)
            dispatch = (combine != 0).astype(logits.dtype)
            return (dispatch, combine)
        key = jax.random.key(seed)
        k0, k1, k2, k3, k4 = jax.random.split(key, 5)
        return {'inputs': jax.random.normal(k0, (B, L, M), jnp.float32), 'router_w': jax.random.normal(k1, (M, E), jnp.float32) * 0.02, 'w0_kernel': jax.random.normal(k2, (E, M, H), jnp.float32) * 0.02, 'w1_kernel': jax.random.normal(k3, (E, M, H), jnp.float32) * 0.02, 'wo_kernel': jax.random.normal(k4, (E, H, M), jnp.float32) * 0.02}
    _L1_ffn_in = _L1_ffn_setup()
    _d = {'L0_attn_x': _L0_attn_in['x'], 'L0_attn_Wq': _L0_attn_in['Wq'], 'L0_attn_bq': _L0_attn_in['bq'], 'L0_attn_Wk': _L0_attn_in['Wk'], 'L0_attn_bk': _L0_attn_in['bk'], 'L0_attn_Wv': _L0_attn_in['Wv'], 'L0_attn_bv': _L0_attn_in['bv'], 'L0_attn_Wr': _L0_attn_in['Wr'], 'L0_attn_br': _L0_attn_in['br'], 'L0_attn_Wo': _L0_attn_in['Wo'], 'L0_attn_bo': _L0_attn_in['bo'], 'L0_ffn_Wr': _L0_ffn_in['Wr'], 'L0_ffn_A': _L0_ffn_in['A'], 'L0_ffn_Bw': _L0_ffn_in['Bw'], 'L1_attn_Wq': _L1_attn_in['Wq'], 'L1_attn_bq': _L1_attn_in['bq'], 'L1_attn_Wk': _L1_attn_in['Wk'], 'L1_attn_bk': _L1_attn_in['bk'], 'L1_attn_Wv': _L1_attn_in['Wv'], 'L1_attn_bv': _L1_attn_in['bv'], 'L1_attn_Wo': _L1_attn_in['Wo'], 'L1_attn_bo': _L1_attn_in['bo'], 'L1_attn_Wd': _L1_attn_in['Wd'], 'L1_attn_bd': _L1_attn_in['bd'], 'L1_attn_Wg': _L1_attn_in['Wg'], 'L1_attn_bg': _L1_attn_in['bg'], 'L1_attn_Wgp': _L1_attn_in['Wgp'], 'L1_attn_bgp': _L1_attn_in['bgp'], 'L1_ffn_router_w': _L1_ffn_in['router_w'], 'L1_ffn_w0_kernel': _L1_ffn_in['w0_kernel'], 'L1_ffn_w1_kernel': _L1_ffn_in['w1_kernel'], 'L1_ffn_wo_kernel': _L1_ffn_in['wo_kernel']}
    _x0 = _d['L0_attn_x']
    _d['L0_attn_x'] = jax.random.normal(jax.random.fold_in(jax.random.key(seed), 1), (8, 512, 128), dtype=_x0.dtype)
    del _x0
    return _d

def reference(L0_attn_x, L0_attn_Wq, L0_attn_bq, L0_attn_Wk, L0_attn_bk, L0_attn_Wv, L0_attn_bv, L0_attn_Wr, L0_attn_br, L0_attn_Wo, L0_attn_bo, L0_ffn_Wr, L0_ffn_A, L0_ffn_Bw, L1_attn_Wq, L1_attn_bq, L1_attn_Wk, L1_attn_bk, L1_attn_Wv, L1_attn_bv, L1_attn_Wo, L1_attn_bo, L1_attn_Wd, L1_attn_bd, L1_attn_Wg, L1_attn_bg, L1_attn_Wgp, L1_attn_bgp, L1_ffn_router_w, L1_ffn_w0_kernel, L1_ffn_w1_kernel, L1_ffn_wo_kernel):

    def _L0_attn_ref(x, Wq, bq, Wk, bk, Wv, bv, Wr, br, Wo, bo):
        import jax, jax.numpy as jnp
        import numpy as np
        import math
        D_MODEL = 128
        N_HEADS = 16
        HEAD_DIM = D_MODEL // N_HEADS
        ROT_DIM = min(32, D_MODEL // 4)

        def _xavier(key, fan_in, fan_out):
            lim = math.sqrt(6.0 / (fan_in + fan_out))
            return jax.random.uniform(key, (fan_in, fan_out), jnp.float32, -lim, lim)
        B, S, _ = x.shape
        H, Dh, Dr = (N_HEADS, HEAD_DIM, ROT_DIM)
        q = (x @ Wq + bq).reshape(B, S, H, Dh)
        k = (x @ Wk + bk).reshape(B, S, H, Dh)
        v = (x @ Wv + bv).reshape(B, S, H, Dh)
        r = (x @ Wr + br).reshape(B, S, H, Dr)
        q = jnp.concatenate([q, r], axis=-1)
        k = jnp.concatenate([k, r], axis=-1)
        scale = 1.0 / math.sqrt(Dh + Dr)
        scores = jnp.einsum('bqhd,bkhd->bhqk', q * scale, k)
        attn = jax.nn.softmax(scores, axis=-1)
        out = jnp.einsum('bhqk,bkhd->bqhd', attn, v).reshape(B, S, H * Dh)
        return out @ Wo + bo

    def _L0_ffn_ref(x, Wr, A, Bw):
        import jax, jax.numpy as jnp
        import numpy as np
        B, L, H = (8, 256, 128)
        E, K, R = (8, 2, 64)

        def _gates(cls_tok, Wr):
            logits = cls_tok @ Wr.T
            top_vals, top_idx = jax.lax.top_k(logits, K)
            neg_inf = jnp.full_like(logits, -jnp.inf)
            rows = jnp.arange(logits.shape[0])[:, None]
            masked = neg_inf.at[rows, top_idx].set(top_vals)
            return jax.nn.softmax(masked, axis=-1)
        gates = _gates(x[:, 0, :], Wr)
        mid = jnp.einsum('blh,erh->belr', x, A)
        expert_out = jnp.einsum('belr,ehr->belh', mid, Bw)
        weighted = jnp.einsum('be,belh->blh', gates, expert_out)
        return x + weighted

    def _L1_attn_ref(x, Wq, bq, Wk, bk, Wv, bv, Wo, bo, Wd, bd, Wg, bg, Wgp, bgp):
        import jax, jax.numpy as jnp
        import numpy as np
        H = 8
        SPARSITY = 0.1
        B, S, D = x.shape
        Dh = D // H
        scale = Dh ** (-0.5)
        k = max(int(S * SPARSITY), 1)

        def heads(W, b):
            return (x @ W.T + b).reshape(B, S, H, Dh).transpose(0, 2, 1, 3)
        Q, K, V = (heads(Wq, bq), heads(Wk, bk), heads(Wv, bv))
        scores = jnp.einsum('bhqd,bhkd->bhqk', Q, K) * scale
        thr = jax.lax.top_k(scores, k)[0][..., k - 1:k]
        masked = jnp.where(scores >= thr, scores, -jnp.inf)
        probs = jax.nn.softmax(masked, axis=-1)
        attn = jnp.einsum('bhqk,bhkd->bhqd', probs, V)
        attn = attn.transpose(0, 2, 1, 3).reshape(B, S, D)
        g2 = H * H
        distilled = (attn.reshape(-1, g2) @ Wd.T + bd).reshape(B, S, D)
        gate = jax.nn.sigmoid(x.mean(axis=1) @ Wg.T + bg)
        gate = (gate @ Wgp.T + bgp)[:, None, :]
        mixed = gate * distilled + (1.0 - gate) * attn
        return mixed @ Wo.T + bo

    def _L1_ffn_ref(inputs, router_w, w0_kernel, w1_kernel, wo_kernel):
        import jax, jax.numpy as jnp
        import numpy as np
        B, L, M = (4, 256, 128)
        G, E = (8, 8)
        CAP_FACTOR = 2.0

        def _ffn_size(m, widening=8.0):
            f = int(widening * m) * 2 // 3
            return f + (8 - f) % 8
        H = _ffn_size(M)

        def _gating_top2(logits, C):
            Gd, Sd, Ed = logits.shape
            raw = jax.nn.softmax(logits, axis=-1)
            idx1 = jnp.argmax(raw, axis=-1)
            m1 = jax.nn.one_hot(idx1, Ed, dtype=logits.dtype)
            gate1 = jnp.sum(raw * m1, axis=-1)
            rest = raw * (1.0 - m1)
            idx2 = jnp.argmax(rest, axis=-1)
            m2 = jax.nn.one_hot(idx2, Ed, dtype=logits.dtype)
            gate2 = jnp.sum(rest * m2, axis=-1)
            p1 = jnp.cumsum(m1, axis=-2) - m1
            m1 = m1 * (p1 < C).astype(m1.dtype)
            p1 = jnp.sum(p1 * m1, axis=-1)
            m1_flat = jnp.sum(m1, axis=-1)
            m1_count = jnp.sum(m1, axis=-2)
            p2 = jnp.cumsum(m2, axis=-2) - m2 + m1_count[:, None, :]
            m2 = m2 * (p2 < C).astype(m2.dtype)
            p2 = jnp.sum(p2 * m2, axis=-1)
            m2_flat = jnp.sum(m2, axis=-1)
            gate1 = gate1 * m1_flat
            gate2 = gate2 * m2_flat
            c1 = (gate1[..., None] * jax.nn.one_hot(idx1, Ed, dtype=jnp.float32))[..., None] * jax.nn.one_hot(p1.astype(jnp.int32), C, dtype=jnp.float32)[:, :, None, :]
            c2 = (gate2[..., None] * jax.nn.one_hot(idx2, Ed, dtype=jnp.float32))[..., None] * jax.nn.one_hot(p2.astype(jnp.int32), C, dtype=jnp.float32)[:, :, None, :]
            combine = (c1 + c2).astype(logits.dtype)
            dispatch = (combine != 0).astype(logits.dtype)
            return (dispatch, combine)
        Bb, Ll, Mm = inputs.shape
        S = Bb * Ll // G
        x = inputs.reshape(G, S, Mm)
        logits = jnp.einsum('GSM,ME->GSE', x, router_w)
        cap = int(CAP_FACTOR * S / E)
        C = (cap + 3) // 4 * 4
        dispatch, combine = _gating_top2(logits, C)
        expert_inputs = jnp.einsum('GSEC,GSM->EGCM', dispatch, x)
        layer_w0 = jnp.einsum('EGCM,EMH->EGCH', expert_inputs, w0_kernel)
        layer_w1 = jnp.einsum('EGCM,EMH->EGCH', expert_inputs, w1_kernel)
        hidden = jax.nn.gelu(layer_w0, approximate=True) * layer_w1
        expert_outputs = jnp.einsum('EGCH,EHM->EGCM', hidden, wo_kernel)
        out = jnp.einsum('EGCM,GSEC->GSM', expert_outputs, combine)
        return out.reshape(Bb, Ll, Mm)
    x = L0_attn_x
    x = x + _L0_attn_ref(_layernorm(x, axis=-1), L0_attn_Wq, L0_attn_bq, L0_attn_Wk, L0_attn_bk, L0_attn_Wv, L0_attn_bv, L0_attn_Wr, L0_attn_br, L0_attn_Wo, L0_attn_bo)
    x = x + _L0_ffn_ref(_layernorm(x, axis=-1), L0_ffn_Wr, L0_ffn_A, L0_ffn_Bw)
    x = x + _L1_attn_ref(_layernorm(x, axis=-1), L1_attn_Wq, L1_attn_bq, L1_attn_Wk, L1_attn_bk, L1_attn_Wv, L1_attn_bv, L1_attn_Wo, L1_attn_bo, L1_attn_Wd, L1_attn_bd, L1_attn_Wg, L1_attn_bg, L1_attn_Wgp, L1_attn_bgp)
    x = x + _L1_ffn_ref(_layernorm(x, axis=-1), L1_ffn_router_w, L1_ffn_w0_kernel, L1_ffn_w1_kernel, L1_ffn_wo_kernel)
    return x

_drawn_inputs = setup_inputs


def setup_inputs(seed=0):
    import zlib

    import numpy as np

    out = dict(_drawn_inputs(seed))
    spreads = {'L0_attn_bq': (0.0, 0.8),
     'L0_attn_bk': (0.0, 0.8),
     'L0_attn_bv': (0.0, 0.1),
     'L0_attn_br': (0.0, 0.8),
     'L0_attn_bo': (0.0, 0.1),
     'L1_attn_bq': (0.0, 0.8),
     'L1_attn_bk': (0.0, 0.8),
     'L1_attn_bv': (0.0, 0.708),
     'L1_attn_bo': (0.0, 0.1),
     'L1_attn_bd': (0.0, 0.8),
     'L1_attn_bg': (0.0, 0.8),
     'L1_attn_bgp': (0.0, 0.8)}
    factors = {'L1_attn_Wq': 8.0,
     'L1_attn_Wk': 8.0,
     'L1_attn_Wv': 8.0,
     'L1_attn_Wo': 4.433,
     'L1_attn_Wd': 8.0,
     'L1_attn_Wg': 8.0,
     'L1_attn_Wgp': 8.0,
     'L1_ffn_router_w': 8.0,
     'L1_ffn_w0_kernel': 8.0,
     'L1_ffn_w1_kernel': 8.0,
     'L1_ffn_wo_kernel': 8.0}
    for name, (base, spread) in spreads.items():
        noise = np.random.default_rng([zlib.crc32(name.encode()), seed]).standard_normal(out[name].shape)
        drawn = base * np.exp(spread * noise) if base else spread * noise
        out[name] = jnp.asarray(drawn.astype(out[name].dtype))
    for name, factor in factors.items():
        out[name] = (out[name] * factor).astype(out[name].dtype)
    return out
```

```python
from contextlib import ExitStack

import concourse.bass as bass
from concourse import mybir

F32, F16, BF16, U32 = mybir.dt.float32, mybir.dt.float16, mybir.dt.bfloat16, mybir.dt.uint32
ALU = mybir.AluOpType
ACT = mybir.ActivationFunctionType
AX = mybir.AxisListType

B, S, D = 8, 512, 128
NT = S // 128
H0, DH0, DR = 16, 8, 32
SCALE0 = 1.0 / (DH0 + DR) ** 0.5
K0 = 3 * (DH0 + DR)
E0, R0 = 8, 64
H1, DH1 = 8, 16
SCALE1 = DH1 ** -0.5
K1 = 6 * DH1
TOPK = max(int(S * 0.1), 1)
ROUNDS = -(-(TOPK + 1) // 8)
TIE = 2.0 ** -20
G2 = H1 * H1
E1, FH = 8, 688
FC = -(-FH // 128)
FL = FH - 128 * (FC - 1)
CAP = (int(2.0 * S / E1) + 3) // 4 * 4
SLOTS = E1 * CAP
EPS = 1e-5
LEAD = 24
QPARTS, KPARTS = (0, 0, 0, 1, 1, 2), (0, 1, 2, 0, 1, 0)


class Signal:

    def __init__(self, sem):
        self.sem, self.count = sem, 0

    def one(self):
        self.count += 1
        return 1

    def dma(self):
        self.count += 16
        return 16


def layer0_steps():
    out, done, before = [], 0, None

    def maxima(n):
        nonlocal done
        for _ in range(min(n, H0 * NT - done)):
            out.append(("max", done, 0, 0))
            done += 1
            if done % 16 == 0:
                out.append(("maxrow", done // 16 - 1, 0, 0))

    maxima(LEAD)
    for g in range(H0 // 4):
        for kt in range(NT):
            for pair in range(2):
                out.append(("score", g, kt, pair))
                maxima(2)
            if kt == 1 and g > 0:
                out.append(("norm", g - 1, 0, 0))
            if before is not None:
                out.append(("weigh", *before, 0))
                if before[1] == NT - 1:
                    out.append(("evacuate", before[0], 0, 0))
            before = (g, kt)
    return out + [("weigh", *before, 0), ("evacuate", before[0], 0, 0), ("norm", before[0], 0, 0)]


def layer1_steps():
    out, before = [], None
    for g in range(H1 // 4):
        for kt in range(NT):
            for pair in range(2):
                out.append(("score", g, kt, pair))
            if kt == 1 and g > 0:
                out.append(("norm", g - 1, 0, 0))
            if before is not None:
                out.append(("weigh", *before, 0))
                if before[1] == NT - 1:
                    out.append(("evacuate", before[0], 0, 0))
            before = (g, kt)
    out += [("weigh", *before, 0), ("evacuate", before[0], 0, 0), ("norm", before[0], 0, 0)]
    return out


def two_layers(nc, a, out):
    STEPS0, STEPS1 = layer0_steps(), layer1_steps()
    with ExitStack() as ctx:
        def sb(name, shape, dt=F32):
            return ctx.enter_context(nc.sbuf_tensor(name, shape, dt))

        def signal(name):
            return Signal(ctx.enter_context(nc.semaphore(name)))

        parts0_dram = nc.dram_tensor("parts0", (2, 2 + NT, 128, S), F16, kind="Internal").ap()
        parts1_dram = nc.dram_tensor("parts1", (2, 3, 128, S), BF16, kind="Internal").ap()
        ones0_dram = nc.dram_tensor("ones0", (H0, S), F16, kind="Internal").ap()
        ones1_dram = nc.dram_tensor("ones1", (6 * H1 * NT, 128), BF16, kind="Internal").ap()

        wq0, wk0, wv0, wo0 = (sb(n, [D, D]) for n in ("wq0", "wk0", "wv0", "wo0"))
        wr0 = sb("wr0", [D, H0 * DR])
        bias0 = sb("bias0", [D, 2 + NT])
        bv0 = sb("bv0", [D, 1])
        bo0 = sb("bo0", [128, D])
        gate0 = sb("gate0", [D, E0])
        expert0 = sb("expert0", [D, E0, D])
        wq1, wk1, wv1, wo1 = (sb(n, [D, D]) for n in ("wq1", "wk1", "wv1", "wo1"))
        bias1 = sb("bias1", [D, 2])
        bv1 = sb("bv1", [D, 1])
        bo1 = sb("bo1", [128, D])
        wd1 = sb("wd1", [D, D])
        bd1 = sb("bd1", [D, 1])
        wg1 = sb("wg1", [D, G2])
        bg1 = sb("bg1", [G2, 1])
        wgp1 = sb("wgp1", [G2, D])
        bgp1 = sb("bgp1", [D, 1])
        router = sb("router", [D, E1])
        w0 = sb("w0", [D, E1, FC * 128])
        w1 = sb("w1", [D, E1, FC * 128])
        wo = sb("wo", [128, E1, FC, D])

        ident = sb("ident", [128, 128])
        before_me = sb("before_me", [128, 128], BF16)
        ones_bf = sb("ones_bf", [128, 128], BF16)
        onesrow0 = sb("onesrow0", [16, S], F16)
        iota8 = sb("iota8", [128, E1])
        iotas = sb("iotas", [128, SLOTS])
        mhalf = sb("mhalf", [128, NT])

        xin = sb("xin", [128, NT, D])
        xres = sb("xres", [128, NT, D])
        xsum = sb("xsum", [128, NT, D])
        xn = sb("xn", [128, NT, D])
        xnT = sb("xnT", [D, S])
        otok = sb("otok", [128, NT, D])
        oT = sb("oT", [D, S])
        mixT = sb("mixT", [D, S])
        avs = sb("avs", [128, S])
        stats = sb("stats", [128, NT, nc.vector.BN_STATS_DIM])
        mv = sb("mv", [128, NT, nc.vector.BN_AGGR_DIM])
        veps = sb("veps", [128, NT])
        rstd = sb("rstd", [128, NT])
        vaug0 = sb("vaug0", [128, NT, H0, 32])
        vaug1 = sb("vaug1", [128, NT, H1, 32])
        rec = sb("rec", [128, NT, 4])
        mx0 = sb("mx0", [128, H0 * NT])
        nmax0 = sb("nmax0", [16, 4, 128], F16)
        top8 = sb("top8", [128, 2, 8])
        work = sb("work", [128, 2, S])
        edges = sb("edges", [128, 4, H1 * NT])
        tmp32 = sb("tmp32", [128, 2, H1 * NT])
        edge_parts = sb("edge_parts", [2 * H1 * NT, 3, 128], BF16)
        edge_rest = sb("edge_rest", [2 * H1 * NT, 2, 128])
        small = sb("small", [128, 64])
        idx8 = sb("idx8", [128, NT, 8], U32)
        val8 = sb("val8", [128, NT, 8])
        rt = sb("rt", [128, 12, NT, E1])
        rs = sb("rs", [128, 16, NT])
        m12 = sb("m12", [128, NT, 2 * E1], BF16)
        xmean = sb("xmean", [D, 1])
        g64 = sb("g64", [G2, 4])
        gcol = sb("gcol", [D, 1])
        wmix = sb("wmix", [D, D])
        xeT = sb("xeT", [D, SLOTS])
        ye = sb("ye", [CAP, E1, D])

        arena = sb("arena", [128, 12 * 1024])
        q0s = arena[:, 0:4096].bitcast(F16).rearrange("p (h t) -> p h t", h=H0)
        k0s = arena[:, 4096:8192].bitcast(F16).rearrange("p (h t) -> p h t", h=H0)
        dense0 = arena[:, 8192:11264].bitcast(F16).rearrange("p (w i t) -> p w i t", w=2, t=S)
        q1s = arena[:, 0:2048].bitcast(BF16).rearrange("p (h t) -> p h t", h=H1)
        k1s = arena[:, 2048:4096].bitcast(BF16).rearrange("p (h t) -> p h t", h=H1)
        dense1 = arena[:, 4096:5632].bitcast(BF16).rearrange("p (w i t) -> p w i t", w=2, t=S)
        full1 = arena[:, 5632:6656].rearrange("p (w t) -> p w t", w=2)
        rest1 = arena[:, 6656:7680].rearrange("p (w t) -> p w t", w=2)
        comb = arena[:, 0:2048].rearrange("p (u s) -> p u s", u=2)
        disp = arena[:, 2048:4096].rearrange("p (u s) -> p u s", u=2)
        combT = arena[:, 4096:8192].rearrange("p (e s) -> p e s", e=E1)
        hid = arena[:, 8192:8192 + 2 * FC * 128].rearrange("p (u c s) -> p u c s", u=2, c=FC)
        comb2 = arena[:, 9728:10752]
        probs = sb("probs", [128, 4, 2, S])

        PS = ctx.enter_context(nc.psum_tensor("PS", [128, 8, 512], F32))

        w_ready = signal("w_ready")
        const_ready = signal("const_ready")
        pool_step = signal("pool_step")
        zero_ready = signal("zero_ready")
        ones_ready = signal("ones_ready")
        ex0_psum = signal("ex0_psum")
        ex0_ready = signal("ex0_ready")
        go = {n: signal(f"go_{n}") for n in ("sp", "pool", "pe", "act")}
        arrived = signal("arrived")
        x_loaded = signal("x_loaded")
        var_ready = signal("var_ready")
        rstd_ready = signal("rstd_ready")
        xn_ready = signal("xn_ready")
        xnT_psum = signal("xnT_psum")
        xnT_ready = signal("xnT_ready")
        dve_step = signal("dve_step")
        proj0 = signal("proj0")
        hi0 = signal("hi0")
        lo0 = signal("lo0")
        v0_ready = signal("v0_ready")
        parts0_out = signal("parts0_out")
        stack0 = signal("stack0")
        tile_ready = signal("tile_ready")
        tile_maxed = signal("tile_maxed")
        max_psum = signal("max_psum")
        max_negated = signal("max_negated")
        max_row = signal("max_row")
        score0 = signal("score0")
        prob0 = signal("prob0")
        weighed0 = signal("weighed0")
        av_copied = signal("av_copied")
        av_turned = signal("av_turned")
        normed = signal("normed")
        o_turned = signal("o_turned")
        oT_ready = signal("oT_ready")
        y_psum = signal("y_psum")
        xsum_ready = signal("xsum_ready")
        xres_ready = signal("xres_ready")
        gate_row = signal("gate_row")
        gate_psum = signal("gate_psum")
        gate_max = signal("gate_max")
        gate_exp = signal("gate_exp")
        wmix_ready = signal("wmix_ready")
        proj1 = signal("proj1")
        full1_ready = signal("full1_ready")
        parts1_ready = signal("parts1_ready")
        parts1_out = signal("parts1_out")
        stack1 = signal("stack1")
        mean_ready = signal("mean_ready")
        g64_psum = signal("g64_psum")
        g64_exp = signal("g64_exp")
        g64_ready = signal("g64_ready")
        gcol_psum = signal("gcol_psum")
        rank_tile = signal("rank_tile")
        rank_read = signal("rank_read")
        edges_ready = signal("edges_ready")
        edges_psum = signal("edges_psum")
        edge_split = signal("edge_split")
        edge_rows = signal("edge_rows")
        shift1 = signal("shift1")
        above1 = signal("above1")
        exp1 = signal("exp1")
        prob1 = signal("prob1")
        weighed1 = signal("weighed1")
        dist_psum = signal("dist_psum")
        mix_ready = signal("mix_ready")
        logit_psum = signal("logit_psum")
        logit_ready = signal("logit_ready")
        logit_exp = signal("logit_exp")
        m12_ready = signal("m12_ready")
        count_psum = signal("count_psum")
        comb_ready = signal("comb_ready")
        disp_ready = signal("disp_ready")
        disp_used = signal("disp_used")
        combT_psum = signal("combT_psum")
        combT_ready = signal("combT_ready")
        xeT_ready = signal("xeT_ready")
        up_psum = signal("up_psum")
        gate_up = signal("gate_up")
        gelu_ready = signal("gelu_ready")
        hid_ready = signal("hid_ready")
        ye_psum = signal("ye_psum")
        ye_ready = signal("ye_ready")
        out_ready = signal("out_ready")
        out_stored = signal("out_stored")

        of_a_sequence = range(arrived.sem.num, out_stored.sem.num + 1)

        def end_sequence(engine, name):
            engine.drain().then_inc(arrived.sem, 1)
            engine.wait_ge(go[name].sem, 1)
            engine.sem_clear(go[name].sem)

        block = ctx.enter_context(nc.Block())

        def bank(i, n=1):
            return PS[:, i:i + n, :].rearrange("p b f -> p (b f)")

        def turned(i):
            return PS[:, i, :].rearrange("p (t c) -> p t c", t=4)

        @block.sync
        def _(sp):
            loads = [
                (wq0[:], a["L0_attn_Wq"]), (wk0[:], a["L0_attn_Wk"]), (wr0[:], a["L0_attn_Wr"]),
                (wv0[:], a["L0_attn_Wv"]), (bias0[:, 0:1], a["L0_attn_bq"]), (bias0[:, 1:2], a["L0_attn_bk"]),
                (bias0[:, 2:], a["L0_attn_br"]),
                (bv0[:], a["L0_attn_bv"]), (wo0[:], a["L0_attn_Wo"]),
                (bo0[:], a["L0_attn_bo"].broadcast_to([128, D])),
                (gate0[:], a["L0_ffn_Wr"]),
                (xeT[0:R0, :], a["L0_ffn_A"].rearrange("e r h -> r e h")),
                (ye[0:R0, :, :], a["L0_ffn_Bw"].rearrange("e r h -> r e h")),
                (wq1[:], a["L1_attn_Wq"]), (wk1[:], a["L1_attn_Wk"]), (wv1[:], a["L1_attn_Wv"]),
                (wo1[:], a["L1_attn_Wo"]), (bias1[:, 0:1], a["L1_attn_bq"]), (bias1[:, 1:2], a["L1_attn_bk"]),
                (bv1[:], a["L1_attn_bv"]), (bo1[:], a["L1_attn_bo"].broadcast_to([128, D])),
                (bd1[0:G2, :], a["L1_attn_bd"]), (bd1[G2:, :], a["L1_attn_bd"]),
                (wg1[:], a["L1_attn_Wg"]), (bg1[:], a["L1_attn_bg"]),
                (wgp1[:], a["L1_attn_Wgp"]), (bgp1[:], a["L1_attn_bgp"]),
                (router[:], a["L1_ffn_router_w"]),
                (w0[:, :, 0:FH], a["L1_ffn_w0_kernel"].rearrange("e m h -> m e h")),
                (w1[:, :, 0:FH], a["L1_ffn_w1_kernel"].rearrange("e m h -> m e h")),
                (wo[0:FL, :, FC - 1, :], a["L1_ffn_wo_kernel"][:, 128 * (FC - 1):, :].rearrange("e h m -> h e m")),
            ]
            for dst, src in loads:
                sp.dma_start(dst, src).then_inc(w_ready.sem, w_ready.dma())
            for e in range(E1):
                sp.dma_start(wo[:, e, 0:FC - 1, :], a["L1_ffn_wo_kernel"][e, 0:128 * (FC - 1), :]
                             .rearrange("(c h) m -> h c m", h=128)).then_inc(w_ready.sem, w_ready.dma())
            sp.wait_ge(zero_ready.sem, 2)
            sp.wait_ge(pool_step.sem, 2)
            for h in range(2):
                sp.dma_start(wd1[h * G2:(h + 1) * G2, h * G2:(h + 1) * G2], a["L1_attn_Wd"]
                             ).then_inc(w_ready.sem, w_ready.dma())
            sp.dma_start(ones0_dram, onesrow0[:]).then_inc(ones_ready.sem, ones_ready.dma())
            for h in range(2):
                sp.dma_start(ones1_dram[3 * H1 * NT * h:3 * H1 * NT * (h + 1), :], ones_bf[0:3 * H1 * NT, :]
                             ).then_inc(ones_ready.sem, ones_ready.dma())
            sp.wait_ge(ones_ready.sem, 16 * 3)

            with sp.Fori(0, B) as b:
                sp.dma_start(xin[:], a["L0_attn_x"][b].rearrange("(t p) d -> p t d", p=128)
                             ).then_inc(x_loaded.sem, x_loaded.dma())
                sp.wait_ge(hi0.sem, 2 + NT)
                sp.dma_start(parts0_dram[0].rearrange("i p t -> p i t"), dense0[:, 0, :, :]
                             ).then_inc(parts0_out.sem, parts0_out.dma())
                sp.wait_ge(lo0.sem, 2 + NT)
                sp.dma_start(parts0_dram[1].rearrange("i p t -> p i t"), dense0[:, 1, :, :]
                             ).then_inc(parts0_out.sem, parts0_out.dma())
                sp.wait_ge(parts0_out.sem, parts0_out.count)
                for blk, (qp, kp) in enumerate(((0, 0), (0, 1), (1, 0))):
                    for dst, part, own in ((q0s, qp, 0), (k0s, kp, 1)):
                        sp.dma_start(dst[DR * blk:DR * (blk + 1), :, :],
                                     parts0_dram[part, 2:].rearrange("i (h j) t -> j (i h) t", j=DR)
                                     ).then_inc(stack0.sem, stack0.dma())
                        sp.dma_start(dst[3 * DR + DH0 * blk:3 * DR + DH0 * (blk + 1), :, :],
                                     parts0_dram[part, own].rearrange("(h j) t -> j h t", j=DH0)
                                     ).then_inc(stack0.sem, stack0.dma())
                sp.dma_start(k0s[K0:K0 + 1, :, :], ones0_dram.rearrange("(o h) t -> o h t", o=1)
                             ).then_inc(stack0.sem, stack0.dma())
                for g in range(H0 // 4):
                    sp.wait_ge(max_negated.sem, g + 1)
                    sp.dma_start(q0s[K0:K0 + 1, 4 * g:4 * g + 4, :].rearrange("o h (t q) -> o (h t) q", q=128),
                                 nmax0[:, g, :]).then_inc(max_row.sem, max_row.dma())
                sp.wait_ge(parts1_ready.sem, 2)
                sp.dma_start(parts1_dram.rearrange("w i p t -> p w i t"), dense1[:]
                             ).then_inc(parts1_out.sem, parts1_out.dma())
                sp.wait_ge(parts1_out.sem, parts1_out.count)
                for w, dst, order in ((0, q1s, QPARTS), (1, k1s, KPARTS)):
                    for blk, part in enumerate(order):
                        sp.dma_start(dst[DH1 * blk:DH1 * (blk + 1), :, :],
                                     parts1_dram[w, part].rearrange("(h j) t -> j h t", j=DH1)
                                     ).then_inc(stack1.sem, stack1.dma())
                sp.dma_start(k1s[K1:K1 + 6, :, :], ones1_dram.rearrange("(a h c) f -> a h (c f)", a=6, h=H1)
                             ).then_inc(stack1.sem, stack1.dma())
                for part in range(3):
                    sp.wait_ge(edge_split.sem, part + 1)
                    for w in range(2):
                        row = K1 + 3 * w + part
                        sp.dma_start(q1s[row:row + 1, :, :].rearrange("o h (t q) -> o (h t) q", q=128),
                                     edge_parts[32 * w:32 * w + 32, part, :]
                                     ).then_inc(edge_rows.sem, edge_rows.dma())
                sp.wait_ge(out_ready.sem, 1)
                sp.dma_start(out[b].rearrange("(t p) d -> p t d", p=128), xres[:]
                             ).then_inc(out_stored.sem, out_stored.dma())
                sp.wait_ge(out_stored.sem, 16)
                end_sequence(sp, "sp")

        @block.gpsimd
        def _(pool):
            pool.memset(ident[:], 0.0).then_inc(pool_step.sem, 1)
            pool.memset(ones_bf[:], 1.0).then_inc(pool_step.sem, 1)
            pool.wait_ge(pool_step.sem, 2)
            pool.affine_select(out=ident[:], in_=ident[:], compare_op=ALU.not_equal, fill=1.0, base=0,
                               pattern=[[-1, 128]], channel_multiplier=1).then_inc(const_ready.sem, 1)
            pool.affine_select(out=before_me[:], in_=ones_bf[:], compare_op=ALU.is_ge, fill=0.0, base=-1,
                               pattern=[[1, 128]], channel_multiplier=-1).then_inc(const_ready.sem, 1)
            pool.iota(iota8[:], [[1, E1]], base=0, channel_multiplier=0,
                      allow_small_or_imprecise_dtypes=True).then_inc(const_ready.sem, 1)
            pool.iota(iotas[:], [[1, SLOTS]], base=0, channel_multiplier=0,
                      allow_small_or_imprecise_dtypes=True).then_inc(const_ready.sem, 1)
            pool.memset(mhalf[:], -0.5).then_inc(const_ready.sem, 1)
            pool.wait_ge(const_ready.sem, 5)
            pool.wait_ge(w_ready.sem, W_LOADS)

            with pool.Fori(0, B) as b:
                def inverse_root(k):
                    pool.wait_ge(var_ready.sem, k + 1)
                    pool.tensor_tensor(rstd[:], veps[:], mhalf[:], ALU.pow
                                       ).then_inc(rstd_ready.sem, rstd_ready.one())

                inverse_root(0)
                pool.wait_ge(x_loaded.sem, 16)
                for t in range(NT):
                    pool.tensor_tensor(xsum[:, t, :], xin[:, t, :], bo0[:], ALU.add
                                       ).then_inc(xsum_ready.sem, xsum_ready.one())
                inverse_root(1)
                pool.wait_ge(xn_ready.sem, 2)
                pool.tensor_tensor(xsum[:], xres[:], xn[:], ALU.add).then_inc(xsum_ready.sem, xsum_ready.one())
                inverse_root(2)
                for t in range(NT):
                    pool.tensor_tensor(xsum[:, t, :], xres[:, t, :], bo1[:], ALU.add
                                       ).then_inc(xsum_ready.sem, xsum_ready.one())
                inverse_root(3)
                end_sequence(pool, "pool")

        @block.tensor
        def _(pe):
            pe.wait_ge(w_ready.sem, W_LOADS)
            pe.wait_ge(const_ready.sem, 5)
            pe.wait_ge(zero_ready.sem, ZEROS)
            for e in range(E0):
                mm = pe.matmul(turned(e // 4)[:, e % 4, :], xeT[0:R0, e * D:(e + 1) * D], ye[0:R0, e, :],
                               start=True, stop=True)
            mm.then_inc(ex0_psum.sem, 1)
            pe.wait_ge(ex0_ready.sem, 1)

            with pe.Fori(0, B) as b:
                def turn(src, ready, to):
                    for t in range(NT):
                        mm = pe.transpose(turned(to)[:, t, :], src[:, t, :], ident[:])
                    mm.then_inc(ready.sem, ready.one())

                def turn_normed(k):
                    pe.wait_ge(xn_ready.sem, k + 1)
                    turn(xn, xnT_psum, 7)
                    pe.wait_ge(xnT_ready.sem, k + 1)

                def by_tokens(to, lhsT, rhs, ready):
                    for t in range(NT):
                        mm = pe.matmul(turned(to)[:, t, :], lhsT[:, t * 128:(t + 1) * 128], rhs, start=True, stop=True)
                    mm.then_inc(ready.sem, ready.one())

                turn_normed(0)
                ws = [wq0[:], wk0[:]] + [wr0[:, c * 128:(c + 1) * 128] for c in range(NT)]
                for i, w in enumerate(ws):
                    pe.matmul(bank(i), w, xnT[:], start=True, stop=True).then_inc(proj0.sem, proj0.one())
                by_tokens(6, xnT, wv0[:], proj0)
                pe.wait_ge(stack0.sem, 16 * 13)
                pe.wait_ge(lo0.sem, 2 + NT)
                pe.wait_ge(v0_ready.sem, 1)
                w = 0
                free7 = None
                for what, g, kt, pair in STEPS0:
                    if what == "max":
                        h, qt = divmod(g, NT)
                        if g >= 2:
                            pe.wait_ge(tile_maxed.sem, g - 1)
                        pe.matmul(bank(g % 2), q0s[0:K0, h, qt * 128:(qt + 1) * 128], k0s[0:K0, h, :],
                                  start=True, stop=True).then_inc(tile_ready.sem, tile_ready.one())
                    elif what == "maxrow":
                        pe.wait_ge(tile_maxed.sem, 16 * (g + 1))
                        if free7:
                            pe.wait_ge(free7[0].sem, free7[1])
                        pe.transpose(PS[0:16, 7, 0:128], mx0[:, 16 * g:16 * g + 16], ident[:]
                                     ).then_inc(max_psum.sem, max_psum.one())
                        free7 = (max_negated, g + 1)
                    elif what == "score":
                        if kt == 0 and pair == 0:
                            pe.wait_ge(max_row.sem, 16 * (g + 1))
                        if w >= 2:
                            pe.wait_ge(prob0.sem, w - 1)
                        for i in range(2):
                            h = 4 * g + 2 * pair + i
                            mm = pe.matmul(bank(2 + 2 * (w % 2) + i), k0s[0:K0 + 1, h, kt * 128:(kt + 1) * 128],
                                           q0s[0:K0 + 1, h, :], start=True, stop=True)
                        mm.then_inc(score0.sem, score0.one())
                        w += 1
                    elif what == "weigh":
                        first = 8 * g + 2 * kt
                        pe.wait_ge(prob0.sem, first + 2)
                        if kt == 0 and g > 0:
                            pe.wait_ge(av_copied.sem, g)
                        for i in range(4):
                            mm = pe.matmul(PS[32 * i:32 * i + 32, 6, :], vaug0[:, kt, 4 * g + i, :],
                                           probs[:, (first + i // 2) % 4, i % 2, :],
                                           start=(kt == 0), stop=(kt == NT - 1))
                        mm.then_inc(weighed0.sem, weighed0.one())
                    elif what == "norm":
                        pe.wait_ge(av_copied.sem, g + 1)
                        if free7:
                            pe.wait_ge(free7[0].sem, free7[1])
                        for t in range(NT):
                            mm = pe.transpose(turned(7)[:, t, :], avs[:, t * 128:(t + 1) * 128], ident[:])
                        mm.then_inc(av_turned.sem, av_turned.one())
                        free7 = (normed, g + 1)
                pe.wait_ge(normed.sem, H0 // 4)
                turn(otok, o_turned, 7)
                pe.wait_ge(oT_ready.sem, 1)
                by_tokens(6, oT, wo0[:], y_psum)
                turn_normed(1)
                pe.wait_ge(gate_row.sem, 1)
                pe.matmul(PS[:, 7, 0:E0], mixT[:, 0:128], gate0[:], start=True, stop=True
                          ).then_inc(gate_psum.sem, gate_psum.one())
                pe.wait_ge(wmix_ready.sem, 1)
                by_tokens(6, xnT, wmix[:], y_psum)
                turn_normed(2)
                pe.matmul(bank(0), wq1[:], xnT[:], start=True, stop=True).then_inc(proj1.sem, proj1.one())
                pe.matmul(bank(1), wk1[:], xnT[:], start=True, stop=True).then_inc(proj1.sem, proj1.one())
                by_tokens(2, xnT, wv1[:], proj1)
                pe.wait_ge(mean_ready.sem, 1)
                pe.matmul(PS[0:G2, 3, 0:1], wg1[:], xmean[:], start=True, stop=True
                          ).then_inc(g64_psum.sem, g64_psum.one())
                pe.wait_ge(g64_ready.sem, 1)
                pe.matmul(PS[:, 3, 8:9], wgp1[:], g64[:, 2:3], start=True, stop=True
                          ).then_inc(gcol_psum.sem, gcol_psum.one())
                pe.wait_ge(stack1.sem, 16 * 13)
                pe.wait_ge(full1_ready.sem, 2)
                for i in range(H1 * NT):
                    h, qt = divmod(i, NT)
                    if i >= 2:
                        pe.wait_ge(rank_read.sem, i - 1)
                    pe.matmul(bank(i % 2), q1s[0:K1, h, qt * 128:(qt + 1) * 128], k1s[0:K1, h, :],
                              start=True, stop=True).then_inc(rank_tile.sem, rank_tile.one())
                pe.wait_ge(edges_ready.sem, 1)
                pe.transpose(PS[0:64, 7, 0:128], edges[:, 0:2, :].rearrange("p w i -> p (w i)"), ident[:]
                             ).then_inc(edges_psum.sem, edges_psum.one())
                pe.wait_ge(edge_rows.sem, 96)
                w = z = 0
                for what, g, kt, pair in STEPS1:
                    if what == "score":
                        if w >= 2:
                            pe.wait_ge(exp1.sem, w - 1)
                        for i in range(2):
                            h = 4 * g + 2 * pair + i
                            mm = pe.matmul(bank(2 + 2 * (w % 2) + i), k1s[0:K1 + 3, h, kt * 128:(kt + 1) * 128],
                                           q1s[0:K1 + 3, h, :], start=True, stop=True)
                        mm.then_inc(shift1.sem, shift1.one())
                        w += 1
                        for i in range(2):
                            h = 4 * g + 2 * pair + i
                            if z >= 2:
                                pe.wait_ge(prob1.sem, z - 1)
                            pe.matmul(bank(z % 2), k1s[0:K1 + 6, h, kt * 128:(kt + 1) * 128],
                                      q1s[0:K1 + 6, h, :], start=True, stop=True
                                      ).then_inc(above1.sem, above1.one())
                            z += 1
                    elif what == "weigh":
                        first = 8 * g + 2 * kt
                        pe.wait_ge(prob1.sem, 2 * (first + 2))
                        if kt == 0:
                            pe.wait_ge(av_copied.sem, H0 // 4 + g)
                        for i in range(4):
                            mm = pe.matmul(PS[32 * i:32 * i + 32, 6, :], vaug1[:, kt, 4 * g + i, :],
                                           probs[:, (first + i // 2) % 4, i % 2, :],
                                           start=(kt == 0), stop=(kt == NT - 1))
                        mm.then_inc(weighed1.sem, weighed1.one())
                    elif what == "norm":
                        pe.wait_ge(av_copied.sem, H0 // 4 + g + 1)
                        pe.wait_ge(normed.sem, H0 // 4 + g)
                        for t in range(NT):
                            mm = pe.transpose(turned(7)[:, t, :], avs[:, t * 128:(t + 1) * 128], ident[:])
                        mm.then_inc(av_turned.sem, av_turned.one())
                pe.wait_ge(normed.sem, H0 // 4 + H1 // 4)
                turn(otok, o_turned, 7)
                pe.wait_ge(oT_ready.sem, 2)
                pe.matmul(bank(5), wd1[:], oT[:], start=True, stop=True).then_inc(dist_psum.sem, dist_psum.one())
                pe.wait_ge(mix_ready.sem, 1)
                by_tokens(6, mixT, wo1[:], y_psum)
                turn_normed(3)
                for t in range(NT):
                    mm = pe.matmul(PS[:, 7, t * E1:(t + 1) * E1], xnT[:, t * 128:(t + 1) * 128], router[:],
                                   start=True, stop=True)
                mm.then_inc(logit_psum.sem, logit_psum.one())
                pe.wait_ge(m12_ready.sem, 1)
                for t in range(NT + 1):
                    col = PS[:, 7, 64 + 16 * t:80 + 16 * t]
                    if t:
                        for s in range(t):
                            mm = pe.matmul(col, ones_bf[:], m12[:, s, :], start=(s == 0), stop=(t == NT and s == t - 1))
                    if t < NT:
                        mm = pe.matmul(col, before_me[:], m12[:, t, :], start=(t == 0), stop=True)
                mm.then_inc(count_psum.sem, count_psum.one())
                for t in range(NT):
                    pe.wait_ge(comb_ready.sem, t + 1)
                    for half in range(2):
                        if 2 * t + half >= 1:
                            pe.wait_ge(combT_ready.sem, 2 * t + half)
                        for e in range(4):
                            c = (4 * half + e) * CAP
                            mm = pe.transpose(turned(6)[:, e, :], comb[:, t % 2, c:c + CAP], ident[:])
                        mm.then_inc(combT_psum.sem, combT_psum.one())
                    pe.wait_ge(disp_ready.sem, t + 1)
                    for half in range(2):
                        mm = pe.matmul(bank(4 + half), xn[:, t, :], disp[:, t % 2, half * 512:(half + 1) * 512],
                                       start=(t == 0), stop=(t == NT - 1))
                    mm.then_inc(disp_used.sem, disp_used.one())
                pe.wait_ge(xeT_ready.sem, 2)

                def down(e):
                    pe.wait_ge(hid_ready.sem, e + 1)
                    if e >= 2:
                        pe.wait_ge(ye_ready.sem, e - 1)
                    for c in range(FC):
                        n = 128 if c < FC - 1 else FL
                        mm = pe.matmul(PS[:, 4 + e % 2, 0:D], hid[0:n, e % 2, c, :], wo[0:n, e, c, :],
                                       start=(c == 0), stop=(c == FC - 1))
                    mm.then_inc(ye_psum.sem, ye_psum.one())

                for e in range(E1):
                    for at, weights, freed, ready in ((0, w0, gelu_ready, up_psum), (2, w1, hid_ready, gate_up)):
                        if e >= 1:
                            pe.wait_ge(freed.sem, e)
                        for c in range(FC):
                            mm = pe.matmul(bank(at, 2)[:, c * 128:(c + 1) * 128], weights[:, e, c * 128:(c + 1) * 128],
                                           xeT[:, e * CAP:(e + 1) * CAP], start=True, stop=True)
                        mm.then_inc(ready.sem, ready.one())
                        if at == 0 and e >= 1:
                            down(e - 1)
                down(E1 - 1)
                pe.wait_ge(ye_ready.sem, E1)
                for t in range(NT):
                    for e in range(E1):
                        mm = pe.matmul(turned(7)[:, t, :], combT[:, e, t * 128:(t + 1) * 128], ye[:, e, :],
                                       start=(e == 0), stop=(e == E1 - 1))
                mm.then_inc(y_psum.sem, y_psum.one())
                end_sequence(pe, "pe")

        @block.scalar
        def _(act):
            act.wait_ge(w_ready.sem, W_LOADS)
            act.wait_ge(ex0_psum.sem, 1)
            act.activation(expert0[:].rearrange("p e h -> p (e h)"), bank(0, 2), ACT.Identity
                           ).then_inc(ex0_ready.sem, 1)

            with act.Fori(0, B) as b:
                def evacuate_turned(k):
                    act.wait_ge(xnT_psum.sem, k + 1)
                    act.activation(xnT[:], bank(7), ACT.Identity).then_inc(xnT_ready.sem, xnT_ready.one())

                evacuate_turned(0)
                for i in range(2 + NT):
                    act.wait_ge(proj0.sem, i + 1)
                    act.activation(dense0[:, 0, i, :], bank(i), ACT.Identity, bias=bias0[:, i:i + 1]
                                   ).then_inc(hi0.sem, hi0.one())
                act.wait_ge(proj0.sem, 3 + NT)
                act.activation(vaug0[:, :, :, 0:DH0],
                               PS[:, 6, :].rearrange("p (t h d) -> p t h d", t=NT, h=H0), ACT.Identity
                               ).then_inc(v0_ready.sem, v0_ready.one())
                w = 0
                for what, g, kt, pair in STEPS0:
                    if what == "maxrow":
                        act.wait_ge(max_psum.sem, g + 1)
                        act.activation(nmax0[:, g, :], PS[0:16, 7, 0:128], ACT.Identity, scale=-1.0
                                       ).then_inc(max_negated.sem, max_negated.one())
                    elif what == "score":
                        act.wait_ge(score0.sem, w + 1)
                        if w >= 4:
                            act.wait_ge(weighed0.sem, (w - 4) // 2 + 1)
                        act.activation(probs[:, w % 4, :, :].rearrange("p i q -> p (i q)"),
                                       bank(2 + 2 * (w % 2), 2), ACT.Exp, scale=SCALE0
                                       ).then_inc(prob0.sem, prob0.one())
                        w += 1
                    elif what == "evacuate":
                        act.wait_ge(weighed0.sem, NT * (g + 1))
                        if g >= 1:
                            act.wait_ge(av_turned.sem, g)
                        act.activation(avs[:], bank(6), ACT.Identity).then_inc(av_copied.sem, av_copied.one())
                act.wait_ge(o_turned.sem, 1)
                act.activation(oT[:], bank(7), ACT.Identity, bias=bv0[:, 0:1]).then_inc(oT_ready.sem, oT_ready.one())
                evacuate_turned(1)
                act.wait_ge(gate_max.sem, 1)
                act.activation(small[:, 8:16], PS[:, 7, 0:E0], ACT.Exp, bias=small[:, 16:17]
                               ).then_inc(gate_exp.sem, gate_exp.one())
                evacuate_turned(2)
                for w in range(2):
                    act.wait_ge(proj1.sem, w + 1)
                    act.activation(full1[:, w, :], bank(w), ACT.Identity, bias=bias1[:, w:w + 1]
                                   ).then_inc(full1_ready.sem, full1_ready.one())
                act.wait_ge(proj1.sem, 3)
                act.activation(vaug1[:, :, :, 0:DH1],
                               PS[:, 2, :].rearrange("p (t h d) -> p t h d", t=NT, h=H1), ACT.Identity
                               ).then_inc(full1_ready.sem, full1_ready.one())
                act.wait_ge(g64_psum.sem, 1)
                act.activation(g64[:, 0:1], PS[0:G2, 3, 0:1], ACT.Exp, bias=bg1[:, 0:1], scale=-1.0 / S
                               ).then_inc(g64_exp.sem, g64_exp.one())
                w = 0
                for what, g, kt, pair in STEPS1:
                    if what == "score":
                        act.wait_ge(shift1.sem, w + 1)
                        if w >= 4:
                            act.wait_ge(weighed1.sem, (w - 4) // 2 + 1)
                        act.activation(probs[:, w % 4, :, :].rearrange("p i q -> p (i q)"),
                                       bank(2 + 2 * (w % 2), 2), ACT.Exp, scale=SCALE1
                                       ).then_inc(exp1.sem, exp1.one())
                        w += 1
                    elif what == "evacuate":
                        act.wait_ge(weighed1.sem, NT * (g + 1))
                        act.wait_ge(av_turned.sem, H0 // 4 + g)
                        act.activation(avs[:], bank(6), ACT.Identity).then_inc(av_copied.sem, av_copied.one())
                act.wait_ge(o_turned.sem, 2)
                act.activation(oT[:], bank(7), ACT.Identity, bias=bv1[:, 0:1]).then_inc(oT_ready.sem, oT_ready.one())
                evacuate_turned(3)
                act.wait_ge(logit_ready.sem, 1)
                act.activation(rt[:, 1, :, :], rt[:, 0, :, :], ACT.Exp).then_inc(logit_exp.sem, logit_exp.one())
                for t in range(NT):
                    for half in range(2):
                        act.wait_ge(combT_psum.sem, 2 * t + half + 1)
                        act.activation(combT[:, 4 * half:4 * half + 4, t * 128:(t + 1) * 128], turned(6),
                                       ACT.Identity).then_inc(combT_ready.sem, combT_ready.one())
                act.wait_ge(disp_used.sem, NT)
                for half in range(2):
                    act.activation(xeT[:, half * 512:(half + 1) * 512], bank(4 + half), ACT.Identity
                                   ).then_inc(xeT_ready.sem, xeT_ready.one())

                def copy_ye(e):
                    act.wait_ge(ye_psum.sem, e + 1)
                    act.activation(ye[:, e, :], PS[:, 4 + e % 2, 0:D], ACT.Identity
                                   ).then_inc(ye_ready.sem, ye_ready.one())

                for e in range(E1):
                    act.wait_ge(up_psum.sem, e + 1)
                    if e >= 2:
                        act.wait_ge(ye_psum.sem, e - 1)
                    act.activation(hid[:, e % 2, :, :].rearrange("p c s -> p (c s)"), bank(0, 2)[:, 0:FC * 128],
                                   ACT.Gelu_apprx_tanh).then_inc(gelu_ready.sem, gelu_ready.one())
                    if e >= 1:
                        copy_ye(e - 1)
                copy_ye(E1 - 1)
                end_sequence(act, "act")

        @block.vector
        def _(dve):
            dve.memset(wd1[:], 0.0).then_inc(zero_ready.sem, 1)
            dve.memset(onesrow0[:], 1.0).then_inc(zero_ready.sem, 1)
            dve.memset(w0[:, :, FH:], 0.0).then_inc(zero_ready.sem, 1)
            dve.memset(w1[:, :, FH:], 0.0).then_inc(zero_ready.sem, 1)
            dve.memset(vaug0[:, :, :, DH0 + 1:], 0.0).then_inc(zero_ready.sem, 1)
            dve.memset(vaug0[:, :, :, DH0:DH0 + 1], 1.0).then_inc(zero_ready.sem, 1)
            dve.memset(vaug1[:, :, :, DH1 + 1:], 0.0).then_inc(zero_ready.sem, 1)
            dve.memset(vaug1[:, :, :, DH1:DH1 + 1], 1.0).then_inc(zero_ready.sem, 1)
            dve.wait_ge(w_ready.sem, W_LOADS)
            dve.tensor_scalar(bg1[:], bg1[:], -1.0, None, ALU.mult).then_inc(zero_ready.sem, 1)
            dve.wait_ge(const_ready.sem, 5)

            with dve.Fori(0, B) as b:
                def step(ins):
                    ins.then_inc(dve_step.sem, dve_step.one())
                    dve.wait_ge(dve_step.sem, dve_step.count)

                def loose(ins):
                    ins.then_inc(dve_step.sem, dve_step.one())

                def settle():
                    dve.wait_ge(dve_step.sem, dve_step.count)

                def layernorm(k, x):
                    settle()
                    for t in range(NT):
                        loose(dve.bn_stats(stats[:, t, :], x[:, t, :]))
                    settle()
                    for t in range(NT):
                        loose(dve.bn_aggr(mv[:, t, :], stats[:, t, :]))
                    settle()
                    dve.tensor_scalar(veps[:], mv[:, :, 1], EPS, None, ALU.add
                                      ).then_inc(var_ready.sem, var_ready.one())
                    dve.wait_ge(rstd_ready.sem, k + 1)
                    for t in range(NT):
                        ins = dve.tensor_scalar(xn[:, t, :], x[:, t, :], mv[:, t, 0:1], rstd[:, t:t + 1],
                                                ALU.subtract, ALU.mult)
                    ins.then_inc(xn_ready.sem, xn_ready.one())

                def add_residual(k, summed, at, ready, to=xres):
                    dve.wait_ge(xsum_ready.sem, summed)
                    dve.wait_ge(y_psum.sem, k + 1)
                    dve.tensor_tensor(to[:].rearrange("p t d -> p (t d)"), bank(at),
                                      xsum[:].rearrange("p t d -> p (t d)"), ALU.add).then_inc(ready.sem, ready.one())
                    dve.wait_ge(ready.sem, ready.count)

                def normalise(g, per, done):
                    dve.wait_ge(av_turned.sem, done)
                    av = PS[:, 7, :].rearrange("p (t i c) -> p t i c", t=NT, i=4)
                    step(dve.reciprocal(rec[:], av[:, :, :, per]))
                    o = otok[:, :, 4 * g * per:4 * (g + 1) * per].rearrange("p t (i c) -> p t i c", i=4)
                    dve.tensor_tensor(o, av[:, :, :, 0:per], rec[:].unsqueeze(3).broadcast_to([128, NT, 4, per]),
                                      ALU.mult).then_inc(normed.sem, normed.one())

                dve.wait_ge(x_loaded.sem, 16)
                layernorm(0, xin)
                for i in range(2 + NT):
                    dve.wait_ge(hi0.sem, i + 1)
                    dve.scalar_tensor_tensor(dense0[:, 1, i, :], bank(i), bias0[:, i:i + 1], dense0[:, 0, i, :],
                                             ALU.add, ALU.subtract).then_inc(lo0.sem, lo0.one())
                for what, g, kt, pair in STEPS0:
                    if what == "max":
                        dve.wait_ge(tile_ready.sem, g + 1)
                        dve.tensor_reduce(mx0[:, g:g + 1], bank(g % 2), AX.X, ALU.max
                                          ).then_inc(tile_maxed.sem, tile_maxed.one())
                    elif what == "norm":
                        normalise(g, DH0, g + 1)
                add_residual(0, NT, 6, xres_ready)
                layernorm(1, xres)
                dve.wait_ge(xnT_ready.sem, 2)
                dve.tensor_copy(mixT[:, 0:128], xnT[:, 0:1].broadcast_to([D, 128])
                                ).then_inc(gate_row.sem, gate_row.one())
                dve.wait_ge(gate_psum.sem, 1)
                step(dve.tensor_copy(small[:, 0:8], PS[:, 7, 0:E0]))
                step(dve.max(val8[:, 0, :], small[:, 0:8]))
                dve.tensor_scalar(small[:, 16:17], val8[:, 0, 0:1], -1.0, None, ALU.mult
                                  ).then_inc(gate_max.sem, gate_max.one())
                step(dve.max_index(idx8[:, 0, :], val8[:, 0, :], small[:, 0:8]))
                step(dve.tensor_copy(small[:, 24:26], idx8[:, 0, 0:2]))
                step(dve.tensor_scalar(small[:, 32:40], iota8[:], small[:, 24:25], None, ALU.is_equal))
                step(dve.scalar_tensor_tensor(small[:, 40:48], iota8[:], small[:, 25:26], small[:, 32:40],
                                              ALU.is_equal, ALU.add))
                dve.wait_ge(gate_exp.sem, 1)
                step(dve.tensor_tensor(small[:, 32:40], small[:, 8:16], small[:, 40:48], ALU.mult))
                step(dve.tensor_reduce(small[:, 17:18], small[:, 32:40], AX.X, ALU.add))
                step(dve.reciprocal(small[:, 18:19], small[:, 17:18]))
                step(dve.tensor_scalar(small[:, 48:56], small[:, 32:40], small[:, 18:19], None, ALU.mult))
                step(dve.tensor_scalar(wmix[:], expert0[:, 0, :], small[:, 48:49], None, ALU.mult))
                for e in range(1, E0):
                    ins = dve.scalar_tensor_tensor(wmix[:], expert0[:, e, :], small[:, 48 + e:49 + e], wmix[:],
                                                   ALU.mult, ALU.add)
                    if e < E0 - 1:
                        step(ins)
                ins.then_inc(wmix_ready.sem, wmix_ready.one())
                add_residual(1, NT + 1, 6, xres_ready)
                layernorm(2, xres)
                dve.wait_ge(xnT_ready.sem, 3)
                dve.tensor_reduce(xmean[:], xnT[:], AX.X, ALU.add).then_inc(mean_ready.sem, mean_ready.one())
                for w in range(2):
                    dve.wait_ge(full1_ready.sem, w + 1)
                    step(dve.tensor_copy(dense1[:, w, 0, :], full1[:, w, :]))
                    step(dve.tensor_tensor(rest1[:, w, :], full1[:, w, :], dense1[:, w, 0, :], ALU.subtract))
                    step(dve.tensor_copy(dense1[:, w, 1, :], rest1[:, w, :]))
                    dve.tensor_tensor(dense1[:, w, 2, :], rest1[:, w, :], dense1[:, w, 1, :], ALU.subtract
                                      ).then_inc(parts1_ready.sem, parts1_ready.one())
                dve.wait_ge(g64_exp.sem, 1)
                step(dve.tensor_scalar(g64[:, 1:2], g64[:, 0:1], 1.0, None, ALU.add))
                dve.reciprocal(g64[:, 2:3], g64[:, 1:2]).then_inc(g64_ready.sem, g64_ready.one())
                dve.wait_ge(gcol_psum.sem, 1)
                step(dve.tensor_scalar(gcol[:], PS[:, 3, 8:9], bgp1[:, 0:1], None, ALU.add))
                for i in range(H1 * NT):
                    dve.wait_ge(rank_tile.sem, i + 1)
                    src = bank(i % 2)
                    settle()
                    for r in range(ROUNDS):
                        t8 = top8[:, r % 2, :]
                        step(dve.max(t8, src))
                        if r == 0:
                            loose(dve.tensor_copy(edges[:, 0, i:i + 1], t8[:, 0:1]))
                        if r < ROUNDS - 1:
                            ins = dve.match_replace(work[:, r % 2, :], t8, src, -3.0e38)
                            if r == 0:
                                ins.then_inc(rank_read.sem, rank_read.one())
                                dve.wait_ge(rank_read.sem, rank_read.count)
                                settle()
                            else:
                                step(ins)
                            src = work[:, r % 2, :]
                        else:
                            at = (TOPK - 1) % 8
                            step(dve.tensor_copy(edges[:, 2:4, i:i + 1], t8[:, at:at + 2].unsqueeze(2)))
                step(dve.tensor_tensor(tmp32[:, 0, :], edges[:, 2, :], edges[:, 3, :], ALU.add))
                step(dve.tensor_scalar(tmp32[:, 0, :], tmp32[:, 0, :], 0.5, None, ALU.mult))
                step(dve.scalar_tensor_tensor(tmp32[:, 1, :], edges[:, 2, :], -1.0, edges[:, 0, :],
                                              ALU.mult, ALU.max))
                step(dve.scalar_tensor_tensor(tmp32[:, 1, :], tmp32[:, 1, :], -2.0 * TIE, edges[:, 2, :],
                                              ALU.mult, ALU.add))
                step(dve.tensor_tensor(tmp32[:, 0, :], tmp32[:, 0, :], tmp32[:, 1, :], ALU.min))
                step(dve.tensor_tensor(edges[:, 1, :], edges[:, 0, :], tmp32[:, 0, :], ALU.subtract))
                dve.tensor_scalar(edges[:, 0, :], edges[:, 0, :], -1.0, None, ALU.mult
                                  ).then_inc(edges_ready.sem, edges_ready.one())
                dve.wait_ge(edges_psum.sem, 1)
                rows = PS[0:64, 7, 0:128]
                dve.tensor_copy(edge_parts[:, 0, :], rows).then_inc(edge_split.sem, edge_split.one())
                dve.wait_ge(edge_split.sem, edge_split.count)
                step(dve.tensor_tensor(edge_rest[:, 0, :], rows, edge_parts[:, 0, :], ALU.subtract))
                dve.tensor_copy(edge_parts[:, 1, :], edge_rest[:, 0, :]).then_inc(edge_split.sem, edge_split.one())
                dve.wait_ge(edge_split.sem, edge_split.count)
                dve.tensor_tensor(edge_parts[:, 2, :], edge_rest[:, 0, :], edge_parts[:, 1, :], ALU.subtract
                                  ).then_inc(edge_split.sem, edge_split.one())
                w = z = 0
                for what, g, kt, pair in STEPS1:
                    if what == "score":
                        dve.wait_ge(exp1.sem, w + 1)
                        for i in range(2):
                            dve.wait_ge(above1.sem, z + 1)
                            p = probs[:, w % 4, i, :]
                            dve.scalar_tensor_tensor(p, bank(z % 2), 0.0, p, ALU.is_ge, ALU.mult
                                                     ).then_inc(prob1.sem, prob1.one())
                            z += 1
                        w += 1
                    elif what == "norm":
                        normalise(g, DH1, H0 // 4 + g + 1)
                dve.wait_ge(oT_ready.sem, 2)
                dve.wait_ge(dist_psum.sem, 1)
                step(dve.scalar_tensor_tensor(work[:, 0, :], bank(5), bd1[:, 0:1], oT[:], ALU.add, ALU.subtract))
                dve.scalar_tensor_tensor(mixT[:], work[:, 0, :], gcol[:, 0:1], oT[:], ALU.mult, ALU.add
                                         ).then_inc(mix_ready.sem, mix_ready.one())
                add_residual(2, 2 * NT + 1, 6, xres_ready)
                layernorm(3, xres)
                dve.wait_ge(logit_psum.sem, 1)

                def wide(x):
                    return x.unsqueeze(2).broadcast_to([128, NT, E1])

                def tt(o, x, y, op):
                    step(dve.tensor_tensor(o, x, y, op))

                logits = PS[:, 7, 0:NT * E1].rearrange("p (t e) -> p t e", t=NT)
                step(dve.tensor_reduce(rs[:, 0, :], logits, AX.X, ALU.max))
                dve.tensor_tensor(rt[:, 0, :, :], logits, wide(rs[:, 0, :]), ALU.subtract
                                  ).then_inc(logit_ready.sem, logit_ready.one())
                dve.wait_ge(logit_exp.sem, 1)
                step(dve.tensor_reduce(rs[:, 1, :], rt[:, 1, :, :], AX.X, ALU.add))
                step(dve.reciprocal(rs[:, 2, :], rs[:, 1, :]))
                raw = rt[:, 2, :, :]
                tt(raw, rt[:, 1, :, :], wide(rs[:, 2, :]), ALU.mult)
                for c, src in ((0, raw), (1, rt[:, 3, :, :])):
                    if c:
                        step(dve.tensor_scalar(rt[:, 6, :, :], rt[:, 4, :, :], -1.0, 1.0, ALU.mult, ALU.add))
                        tt(rt[:, 3, :, :], raw, rt[:, 6, :, :], ALU.mult)
                    for t in range(NT):
                        loose(dve.max(val8[:, t, :], src[:, t, :]))
                    settle()
                    for t in range(NT):
                        loose(dve.max_index(idx8[:, t, :], val8[:, t, :], src[:, t, :]))
                    settle()
                    loose(dve.tensor_copy(rs[:, 5 + c, :], val8[:, :, 0]))
                    step(dve.tensor_copy(rs[:, 3 + c, :], idx8[:, :, 0]))
                    tt(rt[:, 4 + c, :, :], iota8[:].unsqueeze(1).broadcast_to([128, NT, E1]),
                       wide(rs[:, 3 + c, :]), ALU.is_equal)
                    ins = dve.tensor_copy(m12[:, :, c * E1:(c + 1) * E1], rt[:, 4 + c, :, :])
                    if c == 0:
                        loose(ins)
                ins.then_inc(m12_ready.sem, m12_ready.one())
                dve.wait_ge(count_psum.sem, 1)
                counts = PS[:, 7, 64:64 + 16 * (NT + 1)].rearrange("p (t c) -> p t c", c=16)
                step(dve.tensor_scalar(small[:, 0:E1], counts[:, NT, 0:E1], float(CAP), None, ALU.min))
                tt(rt[:, 8, :, :], counts[:, 0:NT, E1:2 * E1],
                   small[:, 0:E1].unsqueeze(1).broadcast_to([128, NT, E1]), ALU.add)
                step(dve.tensor_copy(rt[:, 7, :, :], counts[:, 0:NT, 0:E1]))
                for c in range(2):
                    place, chosen = rt[:, 7 + c, :, :], rt[:, 4 + c, :, :]
                    step(dve.tensor_scalar(rt[:, 9, :, :], place, float(CAP), None, ALU.is_lt))
                    tt(rt[:, 9, :, :], rt[:, 9, :, :], chosen, ALU.mult)
                    step(dve.tensor_reduce(rs[:, 9, :], rt[:, 9, :, :], AX.X, ALU.add))
                    tt(rt[:, 10, :, :], place, rt[:, 9, :, :], ALU.mult)
                    step(dve.tensor_reduce(rs[:, 10, :], rt[:, 10, :, :], AX.X, ALU.add))
                    tt(rs[:, 13 + c, :], rs[:, 5 + c, :], rs[:, 9, :], ALU.mult)
                    step(dve.scalar_tensor_tensor(rs[:, 11 + c, :], rs[:, 3 + c, :], float(CAP), rs[:, 10, :],
                                                  ALU.mult, ALU.add))
                for t in range(NT):
                    if t >= 2:
                        dve.wait_ge(combT_psum.sem, 2 * (t - 1))
                        dve.wait_ge(disp_used.sem, t - 1)
                    cm = comb[:, t % 2, :]
                    loose(dve.tensor_scalar(cm, iotas[:], rs[:, 11, t:t + 1], rs[:, 13, t:t + 1],
                                            ALU.is_equal, ALU.mult))
                    step(dve.tensor_scalar(comb2, iotas[:], rs[:, 12, t:t + 1], rs[:, 14, t:t + 1],
                                           ALU.is_equal, ALU.mult))
                    dve.tensor_tensor(cm, cm, comb2, ALU.add).then_inc(comb_ready.sem, comb_ready.one())
                    dve.wait_ge(comb_ready.sem, comb_ready.count)
                    dve.tensor_scalar(disp[:, t % 2, :], cm, 0.0, None, ALU.not_equal
                                      ).then_inc(disp_ready.sem, disp_ready.one())
                for e in range(E1):
                    dve.wait_ge(gelu_ready.sem, e + 1)
                    dve.wait_ge(gate_up.sem, e + 1)
                    h = hid[:, e % 2, :, :].rearrange("p c s -> p (c s)")
                    dve.tensor_tensor(h, bank(2, 2)[:, 0:FC * 128], h, ALU.mult
                                      ).then_inc(hid_ready.sem, hid_ready.one())
                dve.wait_ge(y_psum.sem, 4)
                dve.tensor_tensor(xres[:].rearrange("p t d -> p (t d)"), bank(7),
                                  xres[:].rearrange("p t d -> p (t d)"), ALU.add
                                  ).then_inc(out_ready.sem, out_ready.one())
                dve.drain()
                dve.wait_ge(arrived.sem, len(go))
                dve.sem_clear(of_a_sequence)
                for g in go.values():
                    dve.sem_inc(g.sem, 1)


W_LOADS = 16 * (31 + E1 + 2)
ZEROS = 9

_T = ("L0_ffn_Wr", "L1_attn_Wq", "L1_attn_Wk", "L1_attn_Wv", "L1_attn_Wo", "L1_attn_Wd", "L1_attn_Wg", "L1_attn_Wgp")
_COLS = ("L0_attn_bq", "L0_attn_bk", "L0_attn_bv", "L1_attn_bq", "L1_attn_bk", "L1_attn_bv",
         "L1_attn_bd", "L1_attn_bg", "L1_attn_bgp")
_ROWS = ("L0_attn_bo", "L1_attn_bo")


def build(nc, arrays):
    a = {n: nc.dram_tensor(f"in_{n}", x.shape, mybir.dt.from_np(x.dtype), kind="ExternalInput").ap()
         for n, x in arrays.items()}
    out = nc.dram_tensor("out", (B, S, D), F32, kind="ExternalOutput").ap()
    two_layers(nc, a, out)


def kernel(**inputs):
    import numpy as np
    from concourse import bacc
    from concourse.bass_utils import run_bass_kernel_spmd

    arrays = {}
    for name, x in inputs.items():
        x = np.asarray(x)
        if name in _T:
            x = x.T
        elif name == "L0_ffn_Bw":
            x = x.transpose(0, 2, 1)
        elif name == "L0_attn_br":
            x = x.reshape(-1, 128).T
        elif name in _COLS:
            x = x.reshape(-1, 1)
        elif name in _ROWS:
            x = x.reshape(1, -1)
        arrays[name] = np.ascontiguousarray(x)
    nc = bacc.Bacc("TRN2", target_bir_lowering=False, num_devices=1)
    build(nc, arrays)
    r = run_bass_kernel_spmd(nc, [{f"in_{n}": x for n, x in arrays.items()}], core_ids=[0])
    return r.results[0]["out"]
```
